# Optimizing a Trainium2 kernel written in Bass

```python
import numpy as np
import jax
import jax.numpy as jnp

def _softmax(x, axis=-1):
    return jax.nn.softmax(x, axis=axis)

def _gelu(x):
    return jax.nn.gelu(x, approximate=True)

def _silu(x):
    return jax.nn.silu(x)

def _sigmoid(x):
    return jax.nn.sigmoid(x)

def _layernorm(x, axis=-1, eps=1e-05):
    m = jnp.mean(x, axis=axis, keepdims=True)
    v = jnp.var(x, axis=axis, keepdims=True)
    return (x - m) / jnp.sqrt(v + eps)

def _scatter_add(tgt, idx, src, axis=0):
    return tgt.at[idx].add(src)

def _segment_sum(src, seg, n):
    return jax.ops.segment_sum(src, seg, n)
kernel_name = 'mk_adj_ffn_d1_adj_r2_a5049e'

def setup_inputs(seed: int=0):
    np.random.seed(seed)
    _w = jnp.asarray

    def _rec_inputs():
        import jax
        import jax.numpy as jnp
        _gk = jax.random.key(seed)
        x = -8.776e-05 + 1 * jax.random.normal(jax.random.fold_in(_gk, 1), (10000, 128), jnp.float32)
        _a = jax.random.bernoulli(jax.random.fold_in(_gk, 2), 0.0008, (10000, 10000))
        _a = jnp.logical_or(_a, jnp.swapaxes(_a, -1, -2))
        _a = jnp.logical_or(_a, jnp.eye(10000, dtype=bool))
        _af = _a.astype(jnp.float32)
        _af = _af * jax.random.uniform(jax.random.fold_in(_gk, 3), (10000, 10000), jnp.float32, 0.05, 1)
        adj = _af
        return (x, adj)
    x, adj = _rec_inputs()

    def _L0_gnn_setup():
        import jax, jax.numpy as jnp
        import numpy as np
        N_USER = 10000
        N_ITEM = 10000
        HID = 128
        key = jax.random.key(seed)
        k1, k2, k3, k4, k5, k6, k7 = jax.random.split(key, 7)
        scale = 1.0 / np.sqrt(HID)
        return {'user_feat': jax.random.normal(k1, (N_USER, HID), dtype=jnp.float32), 'item_feat': jax.random.normal(k2, (N_ITEM, HID), dtype=jnp.float32), 'adj': jax.random.uniform(k3, (N_USER, N_ITEM), dtype=jnp.float32), 'W_item': jax.random.uniform(k4, (HID, HID), dtype=jnp.float32, minval=-scale, maxval=scale), 'b_item': jax.random.uniform(k5, (HID,), dtype=jnp.float32, minval=-scale, maxval=scale), 'W_user': jax.random.uniform(k6, (HID, HID), dtype=jnp.float32, minval=-scale, maxval=scale), 'b_user': jax.random.uniform(k7, (HID,), dtype=jnp.float32, minval=-scale, maxval=scale)}
    _L0_gnn_all = _L0_gnn_setup()
    _L0_gnn_in = {k: v for k, v in _L0_gnn_all.items() if k in ('item_feat', 'W_item', 'b_item', 'W_user', 'b_user')}
    del _L0_gnn_all

    def _L0_ffn_setup():
        import jax, jax.numpy as jnp
        import numpy as np
        B, T, D, H, E = (16, 2048, 128, 256, 8)
        key = jax.random.key(seed)
        ks = jax.random.split(key, 5)
        x = jax.random.normal(ks[0], (B, T, D), dtype=jnp.float32)
        gate_w = jax.random.normal(ks[1], (D, E), dtype=jnp.float32) * 0.02
        gate_b = jnp.zeros((E,), dtype=jnp.float32)
        W1 = jax.random.normal(ks[2], (E, D, H), dtype=jnp.float32) * 0.02
        b1 = jnp.zeros((E, H), dtype=jnp.float32)
        W2 = jax.random.normal(ks[3], (E, H, D), dtype=jnp.float32) * 0.02
        b2 = jnp.zeros((E, D), dtype=jnp.float32)
        return {'x': x, 'gate_w': gate_w, 'gate_b': gate_b, 'W1': W1, 'b1': b1, 'W2': W2, 'b2': b2}
    _L0_ffn_all = _L0_ffn_setup()
    _L0_ffn_in = {k: v for k, v in _L0_ffn_all.items() if k in ('gate_w', 'gate_b', 'W1', 'b1', 'W2', 'b2')}
    del _L0_ffn_all
    return {'x': x, 'adj': adj, 'L0_gnn_item_feat': _L0_gnn_in['item_feat'], 'L0_gnn_W_item': _L0_gnn_in['W_item'], 'L0_gnn_b_item': _L0_gnn_in['b_item'], 'L0_gnn_W_user': _L0_gnn_in['W_user'], 'L0_gnn_b_user': _L0_gnn_in['b_user'], 'L0_ffn_gate_w': _L0_ffn_in['gate_w'], 'L0_ffn_gate_b': _L0_ffn_in['gate_b'], 'L0_ffn_W1': _L0_ffn_in['W1'], 'L0_ffn_b1': _L0_ffn_in['b1'], 'L0_ffn_W2': _L0_ffn_in['W2'], 'L0_ffn_b2': _L0_ffn_in['b2']}

def reference(x, adj, L0_gnn_item_feat, L0_gnn_W_item, L0_gnn_b_item, L0_gnn_W_user, L0_gnn_b_user, L0_ffn_gate_w, L0_ffn_gate_b, L0_ffn_W1, L0_ffn_b1, L0_ffn_W2, L0_ffn_b2):
    import jax
    import jax.numpy as jnp

    def _L0_gnn_ref(user_feat, item_feat, adj, W_item, b_item, W_user, b_user):
        import jax, jax.numpy as jnp
        import numpy as np
        N_USER = 10000
        N_ITEM = 10000
        HID = 128
        h = item_feat @ W_item.T + b_item
        b = user_feat @ W_user.T + b_user
        return jax.nn.relu(adj @ h + b)

    def _L0_ffn_ref(x, gate_w, gate_b, W1, b1, W2, b2):
        import jax, jax.numpy as jnp
        import numpy as np
        B, T, D, H, E = (16, 2048, 128, 256, 8)
        Bb, Tt, Dd = x.shape
        Ee = gate_w.shape[1]
        xf = x.reshape(-1, Dd)
        N = xf.shape[0]
        logits = xf @ gate_w + gate_b
        probs = jax.nn.softmax(logits, axis=-1)
        top2_vals, top2_idx = jax.lax.top_k(probs, 2)
        cw = jnp.zeros((N, Ee), dtype=xf.dtype).at[jnp.arange(N)[:, None], top2_idx].add(top2_vals)

        def step(acc, params):
            w1, bb1, w2, bb2, we = params
            h = jax.nn.gelu(xf @ w1 + bb1, approximate=False)
            y = h @ w2 + bb2
            return (acc + we[:, None] * y, None)
        out, _ = jax.lax.scan(step, jnp.zeros_like(xf), (W1, b1, W2, b2, cw.T))
        return out.reshape(Bb, Tt, Dd)
    x = x + _L0_gnn_ref(_layernorm(x, axis=-1), L0_gnn_item_feat, adj, L0_gnn_W_item, L0_gnn_b_item, L0_gnn_W_user, L0_gnn_b_user)
    x = x + _L0_ffn_ref(_layernorm(x, axis=-1)[None], L0_ffn_gate_w, L0_ffn_gate_b, L0_ffn_W1, L0_ffn_b1, L0_ffn_W2, L0_ffn_b2)[0]
    return x

_drawn_inputs = setup_inputs


def setup_inputs(seed=0):
    import zlib

    import numpy as np

    out = dict(_drawn_inputs(seed))
    spreads = {'L0_ffn_gate_b': (0.0, 0.72), 'L0_ffn_b1': (0.0, 0.8), 'L0_ffn_b2': (0.0, 0.535)}
    factors = {'L0_ffn_gate_w': 4.074, 'L0_ffn_W1': 8.0, 'L0_ffn_W2': 8.0}
    for name, (base, spread) in spreads.items():
        noise = np.random.default_rng([zlib.crc32(name.encode()), seed]).standard_normal(out[name].shape)
        drawn = base * np.exp(spread * noise) if base else spread * noise
        out[name] = jnp.asarray(drawn.astype(out[name].dtype))
    for name, factor in factors.items():
        out[name] = (out[name] * factor).astype(out[name].dtype)
    return out
```

```python
import concourse.bass as bass
from concourse import mybir
from concourse.alu_op_type import AluOpType as ALU
from contextlib import ExitStack

F32 = mybir.dt.float32
F32R = mybir.dt.float32r
ACT = mybir.ActivationFunctionType
AX = mybir.AxisListType

P = 128
N_USER, N_ITEM, D, HID, E = 10000, 10000, 128, 256, 8
BLOCKS = 20
UB = N_USER // BLOCKS
SUBS = 4
TS = UB // SUBS
KT = N_ITEM // P
TAIL = N_ITEM - KT * P
KC = 2
CHUNKS = KT // KC
RAW, PARTS = 6, 3
TAILP = 96
HALVES = HID // P
EPS = 1e-5
WPIECE = 1024
FEAT = 3

RELU, X1_T, LN2_BN, LN2_T, Z_SPLIT, GATE = 2, 5, 7, 10, 12, 13
CW_STEP, CW_T = 19, 23
W1_AT = [17, 21] + [22 + 3 * e for e in range(2, E)]
WBC_AT = [26 + 3 * e for e in range(E)]
GELU_AT = [c + 2 for c in W1_AT]
GW_AT = [c + 2 for c in WBC_AT]
SPLIT_AT = [c + 3 for c in WBC_AT]
W2_AT = [c + 5 for c in WBC_AT]
OUT_AT = W2_AT[-1] + 2
LN1_BN, LN1_T = 17, 25
ENDS = 2 * CHUNKS
assert OUT_AT < ENDS

assert KT % KC == 0 and UB % SUBS == 0 and (2 * CHUNKS) % RAW == 0 and CHUNKS % PARTS == 0


def nth(b, per_block, k):
    base, t = b
    v = per_block * base + k
    return v if t is None else v + 2 * per_block * t


def build(nc, adj, adj_tail, x_tok, x_t, feat_t, feat_tail, wi_t, b_item, wu_t, b_user,
          gate_w, gate_b, w1, b1, w2, b2, ident_d, sel_d, tri_d, out):
    ctx = ExitStack()
    with ctx:
        def sb(name, shape, dt=F32):
            return ctx.enter_context(nc.sbuf_tensor("s_" + name, shape, dt))

        def sem(name):
            return ctx.enter_context(nc.semaphore(name))

        raw = sb("raw", [P, RAW, KC * UB])
        a_hi = sb("a_hi", [P, PARTS, KC * UB], F32R)
        a_lo = sb("a_lo", [P, PARTS, KC * UB], F32R)
        tail_raw = sb("tail_raw", [TAILP, UB])
        tail_parts = sb("tail_parts", [TAILP, UB], F32R)
        h_hi = sb("h_hi", [P, KT * D], F32R)
        h_lo = sb("h_lo", [P, KT * D], F32R)
        h_tail = sb("h_tail", [TAILP, D], F32R)
        w1_hi = sb("w1_hi", [P, E * HID], F32R)
        w1_lo = sb("w1_lo", [P, E * HID], F32R)
        w2_hi = sb("w2_hi", [P, E * HALVES * D], F32R)
        w2_lo = sb("w2_lo", [P, E * HALVES * D], F32R)
        b2_hi = sb("b2_hi", [2 * E, D], F32R)
        b2_lo = sb("b2_lo", [2 * E, D], F32R)
        sel = sb("sel", [2 * E, E * P], F32R)
        gw_hi = sb("gatew_hi", [P, E], F32R)
        gw_lo = sb("gatew_lo", [P, E], F32R)
        gatew = sb("gatew", [P, E])
        gateb = sb("gateb", [P, SUBS * E])
        wi = sb("wi", [P, D])
        wu = sb("wu", [P, D])
        bitem = sb("bitem", [P, KC * D])
        buser = sb("buser", [P, 1])
        b1s = sb("b1s", [P, E * HALVES])
        ident = sb("ident", [P, P])
        tri = sb("tri", [P, E, E])
        xtok = sb("xtok", [P, SUBS * D])
        xt = sb("xt", [P, 2, UB])
        relu_ln1 = sb("relu_ln1", [P, 2 * SUBS * E * E])
        lntok = sb("lntok", [P, SUBS * D])
        z_hi = sb("z_hi", [P, UB], F32R)
        z_lo = sb("z_lo", [P, UB], F32R)
        g = sb("g", [P, 2, HALVES * UB])
        gw = sb("gw", [P, WPIECE])
        gwh = sb("gwh", [P, HALVES * UB], F32R)
        gwl = sb("gwl", [P, HALVES * UB], F32R)
        cwt = sb("cwt", [2 * E, UB], F32R)
        y_out = sb("y_out", [P, UB])
        bn6 = sb("bn6", [P, SUBS, 6])
        bn6b = sb("bn6b", [P, SUBS, 6])
        rs1 = sb("rs1", [P, 6, SUBS])
        rs2 = sb("rs2", [P, 6, SUBS])
        consts = sb("consts", [P, 4, SUBS])
        ebase = sb("ebase", [P, SUBS * E])
        col = sb("col", [P, 4, SUBS])
        lg, zz3, ez, pr, rank, cw = (bitem[:, i * SUBS * E:(i + 1) * SUBS * E].rearrange("p (s e) -> p s e", e=E)
                                     for i in range(6))
        zz = bitem[:, SUBS * E:2 * SUBS * E]
        above = relu_ln1[:, 0:SUBS * E * E].rearrange("p (s e f) -> p s e f", e=E, f=E)
        equal = relu_ln1[:, SUBS * E * E:2 * SUBS * E * E].rearrange("p (s e f) -> p s e f", e=E, f=E)
        cwr = sb("cwr", [P, SUBS, 2 * E], F32R)

        def bank(name):
            return ctx.enter_context(nc.psum_tensor("p_" + name, [P, 512], F32))

        agg = [bank("agg0"), bank("agg1")]
        hid = [bank("hid0"), bank("hid1")]
        wbc, y, tp, small = bank("wbc"), bank("y"), bank("tp"), bank("small")

        raw_loaded = [sem(f"raw_loaded{i}") for i in range(RAW)]
        item_loaded, weights_loaded, piece_loaded = sem("item_loaded"), sem("weights_loaded"), sem("piece_loaded")
        feat_loaded = [sem("feat_loaded0"), sem("feat_loaded1")]
        xt_loaded, xtok_loaded, tail_loaded, out_stored = (
            sem("xt_loaded"), sem("xtok_loaded"), sem("tail_loaded"), sem("out_stored"))
        hi_made, lo_made, chunk_used = sem("hi_made"), sem("lo_made"), sem("chunk_used")
        h_prod, h_biased, h_hi_made, h_made = sem("h_prod"), sem("h_biased"), sem("h_hi_made"), sem("h_made")
        piece_hi, piece_split = sem("piece_hi"), sem("piece_split")
        tail_hi, tail_split = sem("tail_hi"), sem("tail_split")
        consts_set = sem("consts_set")
        agg_done, relu_made, x1_made = sem("agg_done"), sem("relu_made"), sem("x1_made")
        x1_transposed, ln2_stats, ln2_rstd, ln2_normed = (
            sem("x1_transposed"), sem("ln2_stats"), sem("ln2_rstd"), sem("ln2_normed"))
        ln2_transposed, z_hi_made, z_split = sem("ln2_transposed"), sem("z_hi_made"), sem("z_split")
        ln1_stats, ln1_normed, ln1_transposed, ln1_copied = (
            sem("ln1_stats"), sem("ln1_normed"), sem("ln1_transposed"), sem("ln1_copied"))
        cwhi_made, ln1_rstd, ln1_scaled = sem("cwhi_made"), sem("ln1_rstd"), sem("ln1_scaled")
        pool_step1, pool_step2 = sem("pool_step1"), sem("pool_step2")
        gate_done, z_made, ez_made, gate_step, cw_made, cw_transposed, cw_ready = (
            sem("gate_done"), sem("z_made"), sem("ez_made"), sem("gate_step"), sem("cw_made"),
            sem("cw_transposed"), sem("cw_ready"))
        hid_ready, gelu_done, wbc_ready, gw_made, gwhi_made, gw_split, w2_done, out_made = (
            sem("hid_ready"), sem("gelu_done"), sem("wbc_ready"), sem("gw_made"), sem("gwhi_made"),
            sem("gw_split"), sem("w2_done"), sem("out_made"))

        NW = 8
        pieces = [(w1_hi, w1_lo, w1, P, 0), (w1_hi, w1_lo, w1, P, WPIECE),
                  (w2_hi, w2_lo, w2, P, 0), (w2_hi, w2_lo, w2, P, WPIECE),
                  (sel, None, sel_d, 2 * E, 0), (b2_hi, b2_lo, b2, 2 * E, 0),
                  (gw_hi, gw_lo, gate_w, P, 0)]
        widths = [WPIECE] * 4 + [E * P, D, E]
        PIECE_AT = [6 + 4 * i for i in range(len(pieces))]
        gstage = g[:, :, :].rearrange("p a n -> p (a n)")
        FW = FEAT * KC * P

        def feat_at(c):
            o = (c // FEAT % 2) * FW + c % FEAT * KC * P
            return gstage[:, o:o + KC * P]

        block = ctx.enter_context(nc.Block())

        @block.sync
        def _(sp):
            def load_raw(b, c):
                s = (CHUNKS * b[0] + c) % RAW
                if not (b[1] is None and CHUNKS * b[0] + c < RAW):
                    sp.wait_ge(lo_made, nth(b, CHUNKS, c - RAW + 1))
                row = b[0] if b[1] is None else b[0] + 2 * b[1]
                src = adj[c, row] if b[1] is None else adj[c, bass.ds(row, 1)].rearrange("a p n -> (a p) n")
                sp.dma_start(raw[:, s, :], src).then_inc(raw_loaded[s], 16)

            def load_block(b):
                start = b[1] is None
                row = b[0] if start else b[0] + 2 * b[1]

                def of(d):
                    return d[row] if start else d[bass.ds(row, 1)].rearrange("a p n -> (a p) n")
                if not (start and b[0] == 0):
                    sp.wait_ge(ln1_normed, nth(b, 1, 0))
                sp.dma_start(xtok[:, :], of(x_tok)).then_inc(xtok_loaded, 16)
                if not (start and b[0] == 0):
                    sp.wait_ge(tail_split, nth(b, 1, 0))
                sp.dma_start(tail_raw[:, :], of(adj_tail)).then_inc(tail_loaded, 16)

            def load_xt(b):
                start = b[1] is None
                row = b[0] if start else b[0] + 2 * b[1]
                if not (start and b[0] < 2):
                    sp.wait_ge(out_made, nth(b, 1, -1))
                if not (start and b[0] == 0):
                    sp.wait_ge(x1_made, nth(b, 1, 0))
                src = x_t[row] if start else x_t[bass.ds(row, 1)].rearrange("a p n -> (a p) n")
                sp.dma_start(xt[:, b[0] % 2, :], src).then_inc(xt_loaded, 16)

            def store_out(b):
                row = b[0] if b[1] is None else b[0] + 2 * b[1]
                dst = out[row] if b[1] is None else out[bass.ds(row, 1)].rearrange("a p n -> (a p) n")
                sp.wait_ge(out_made, nth(b, 1, 1))
                sp.dma_start(dst, y_out[:, 0:UB]).then_inc(out_stored, 16)

            def iteration(b):
                for c in range(CHUNKS):
                    load_raw(b, c)
                    if c == 8:
                        load_block(b)
                    if c == OUT_AT - CHUNKS + 7:
                        load_xt(b)
                        if not (b[1] is None and b[0] < 2):
                            store_out((b[0] - 2, b[1]))

            sp.dma_start(wi[:, :], wi_t).then_inc(item_loaded, 16)
            sp.dma_start(bitem[:, :], b_item).then_inc(item_loaded, 16)
            sp.dma_start(gstage[:, 0:FW], feat_t[0]).then_inc(feat_loaded[0], 16)
            late = [(wu, wu_t), (buser, b_user), (gatew, gate_w), (gateb, gate_b), (b1s, b1),
                    (ident, ident_d)]
            for c in range(CHUNKS):
                load_raw((0, None), c)
                if c % FEAT == 0 and c + FEAT < CHUNKS:
                    k = c // FEAT + 1
                    if k >= 2:
                        sp.wait_ge(h_prod, (k - 1) * FEAT)
                    sp.dma_start(gstage[:, k % 2 * FW:(k % 2 + 1) * FW], feat_t[k])\
                        .then_inc(feat_loaded[k % 2], 16)
                if c == 3:
                    for dst, src in late:
                        sp.dma_start(dst[:, :], src).then_inc(weights_loaded, 16)
                    sp.dma_start(tri[:, :, :], tri_d).then_inc(weights_loaded, 16)
                    sp.dma_start(y_out[:, 0:TAILP], feat_tail).then_inc(weights_loaded, 16)
                for i, (_, _, src, rows, o) in enumerate(pieces):
                    if c == PIECE_AT[i] - 2:
                        if i >= 1:
                            sp.wait_ge(piece_split, i)
                        sp.dma_start(gw[0:rows, 0:widths[i]], src[:, o:o + widths[i]]).then_inc(piece_loaded, 16)
                if c == 8:
                    load_block((0, None))
                if c == OUT_AT - CHUNKS + 7:
                    load_xt((0, None))
            iteration((1, None))
            with sp.Fori(0, (BLOCKS - 2) // 2) as t:
                iteration((2, t))
                iteration((3, t))
            store_out((BLOCKS - 2, None))
            store_out((BLOCKS - 1, None))
            sp.wait_ge(out_stored, 16 * BLOCKS)

        @block.tensor
        def _(pe):
            mm = nc.tensor.matmul

            def h_step(c):
                if c == 0:
                    pe.wait_ge(item_loaded, 16 * 2)
                pe.wait_ge(feat_loaded[c // FEAT % 2], 16 * (c // FEAT // 2 + 1))
                if c >= 2:
                    pe.wait_ge(h_biased, c - 1)
                f = feat_at(c)
                for j in range(KC):
                    last = mm(hid[c % 2][:, j * D:(j + 1) * D], f[:, j * P:(j + 1) * P], wi[:, :],
                              start=True, stop=True)
                last.then_inc(h_prod, 1)

            def h_tail_step():
                pe.wait_ge(weights_loaded, 16 * NW)
                mm(wbc[0:TAILP, 0:D], y_out[:, 0:TAILP], wi[:, :], start=True, stop=True).then_inc(h_prod, 1)

            def agg_chunk(b, c):
                pe.wait_ge(lo_made, nth(b, CHUNKS, c + 1))
                s = c % PARTS
                for j in range(KC):
                    k = c * KC + j
                    hi = a_hi[:, s, j * UB:(j + 1) * UB]
                    lo = a_lo[:, s, j * UB:(j + 1) * UB]
                    hh, hl = h_hi[:, k * D:(k + 1) * D], h_lo[:, k * D:(k + 1) * D]
                    o = agg[b[0] % 2][:, 0:UB]
                    mm(o, hh, hi, start=(k == 0), stop=False)
                    mm(o, hl, hi, start=False, stop=False)
                    last = mm(o, hh, lo, start=False, stop=False)
                last.then_inc(chunk_used, 1)

            def agg_end(b):
                o = agg[b[0] % 2][:, 0:UB]
                pe.wait_ge(tail_split, nth(b, 1, 1))
                mm(o, h_tail[:, :], tail_parts[:, :], start=False, stop=False)
                pe.wait_ge(ln1_copied, nth(b, 1, 1))
                mm(o, wu[:, :], relu_ln1[:, 0:UB], start=False, stop=True).then_inc(agg_done, 1)

            def ln1_turn(b):
                pe.wait_ge(ln1_normed, nth(b, 1, 1))
                for s in range(SUBS):
                    last = nc.tensor.transpose(tp[:, s * TS:(s + 1) * TS],
                                               lntok[0:TS, s * D:(s + 1) * D], ident[0:TS, 0:TS])
                last.then_inc(ln1_transposed, 1)

            def ffn(p, c):
                if c == X1_T:
                    pe.wait_ge(x1_made, nth(p, 1, 1))
                    pe.wait_ge(ln1_copied, nth(p, 1, 1))
                    for s in range(SUBS):
                        last = nc.tensor.transpose(tp[0:TS, s * D:(s + 1) * D],
                                                   xt[:, p[0] % 2, s * TS:(s + 1) * TS], ident[:, :])
                    last.then_inc(x1_transposed, 1)
                if c == LN2_T:
                    pe.wait_ge(ln2_normed, nth(p, 1, 1))
                    for s in range(SUBS):
                        last = nc.tensor.transpose(tp[:, s * TS:(s + 1) * TS],
                                                   lntok[0:TS, s * D:(s + 1) * D], ident[0:TS, 0:TS])
                    last.then_inc(ln2_transposed, 1)
                if c == GATE:
                    pe.wait_ge(z_split, nth(p, 1, 1))
                    if not (p[1] is None and p[0] == 0):
                        pe.wait_ge(cw_ready, nth(p, 1, 0))
                    for s in range(SUBS):
                        o = small[0:TS, s * E:(s + 1) * E]
                        zh, zl = z_hi[:, s * TS:(s + 1) * TS], z_lo[:, s * TS:(s + 1) * TS]
                        mm(o, zh, gw_hi[:, :], start=True, stop=False)
                        mm(o, zh, gw_lo[:, :], start=False, stop=False)
                        last = mm(o, zl, gw_hi[:, :], start=False, stop=True)
                    last.then_inc(gate_done, 1)
                if c == CW_T:
                    pe.wait_ge(cw_made, nth(p, 1, 1))
                    for s in range(SUBS):
                        last = nc.tensor.transpose(small[0:2 * E, s * TS:(s + 1) * TS],
                                                   cwr[0:TS, s, :].bitcast(F32), ident[0:TS, 0:TS])
                    last.then_inc(cw_transposed, 1)
                for e in range(E):
                    if c == W2_AT[e]:
                        if e == 0:
                            if not (p[1] is None and p[0] == 0):
                                pe.wait_ge(out_made, nth(p, 1, 0))
                            mm(y[:, 0:UB], b2_hi[:, :], cwt[:, :], start=True, stop=False)
                            mm(y[:, 0:UB], b2_lo[:, :], cwt[:, :], start=False, stop=False)
                        pe.wait_ge(gw_split, nth(p, E, e + 1))
                        for h in range(HALVES):
                            o = (e * HALVES + h) * D
                            gh, gl = gwh[:, h * UB:(h + 1) * UB], gwl[:, h * UB:(h + 1) * UB]
                            mm(y[:, 0:UB], w2_hi[:, o:o + D], gh, start=False, stop=False)
                            mm(y[:, 0:UB], w2_lo[:, o:o + D], gh, start=False, stop=False)
                            last = mm(y[:, 0:UB], w2_hi[:, o:o + D], gl, start=False,
                                      stop=(e == E - 1 and h == HALVES - 1))
                        last.then_inc(w2_done, 1)
                    if c == WBC_AT[e]:
                        if e == 0:
                            pe.wait_ge(cw_ready, nth(p, 1, 1))
                        if not (p[1] is None and p[0] == 0 and e == 0):
                            pe.wait_ge(gw_made, nth(p, E, e))
                        mm(wbc[:, 0:UB], sel[:, e * P:(e + 1) * P], cwt[:, :], start=True, stop=True)\
                            .then_inc(wbc_ready, 1)
                    if c == W1_AT[e]:
                        if not (p[1] is None and p[0] == 0 and e == 0):
                            pe.wait_ge(gelu_done, nth(p, E, e))
                        for h in range(HALVES):
                            o = e * HID + h * P
                            mm(hid[h][:, 0:UB], w1_hi[:, o:o + P], z_hi[:, :], start=True, stop=False)
                            mm(hid[h][:, 0:UB], w1_lo[:, o:o + P], z_hi[:, :], start=False, stop=False)
                            last = mm(hid[h][:, 0:UB], w1_hi[:, o:o + P], z_lo[:, :], start=False, stop=True)
                        last.then_inc(hid_ready, 1)

            def iteration(b):
                for c in range(CHUNKS):
                    agg_chunk(b, c)
                    if not (b[1] is None and b[0] < 2):
                        ffn((b[0] - 2, b[1]), CHUNKS + c)
                    ffn((b[0] - 1, b[1]), c)
                    if c == LN1_T:
                        pe.wait_ge(z_split, nth(b, 1, 0))
                        ln1_turn(b)
                agg_end(b)

            first = (0, None)
            h_step(0)
            h_step(1)
            for c in range(CHUNKS):
                if c + 2 < CHUNKS:
                    h_step(c + 2)
                if c + 2 == CHUNKS:
                    h_tail_step()
                pe.wait_ge(h_made, c + 1)
                agg_chunk(first, c)
            ln1_turn(first)
            pe.wait_ge(h_made, CHUNKS + 1)
            pe.wait_ge(piece_split, len(pieces))
            agg_end(first)
            iteration((1, None))
            with pe.Fori(0, (BLOCKS - 2) // 2) as t:
                iteration((2, t))
                iteration((3, t))
            for c in range(CHUNKS):
                ffn((BLOCKS - 2, None), CHUNKS + c)
                ffn((BLOCKS - 1, None), c)
            for c in range(CHUNKS, ENDS):
                ffn((BLOCKS - 1, None), c)

        @block.scalar
        def _(act):
            fn = nc.scalar.activation

            def hi_chunk(b, c):
                n = CHUNKS * b[0] + c
                act.wait_ge(raw_loaded[n % RAW], 16 * (n // RAW + 1) if b[1] is None
                            else 16 * (n // RAW + 1) + 16 * (2 * CHUNKS // RAW) * b[1])
                if not (b[1] is None and n < PARTS):
                    act.wait_ge(chunk_used, nth(b, CHUNKS, c - PARTS + 1))
                fn(a_hi[:, c % PARTS, :], raw[:, n % RAW, :], ACT.Copy).then_inc(hi_made, 1)

            def tail_round(b):
                act.wait_ge(tail_loaded, nth(b, 16, 16))
                if not (b[1] is None and b[0] == 0):
                    act.wait_ge(agg_done, nth(b, 1, 0))
                fn(tail_parts[:, :], tail_raw[:, :], ACT.Copy).then_inc(tail_hi, 1)

            def ln1_copy(b):
                act.wait_ge(ln1_transposed, nth(b, 1, 1))
                if not (b[1] is None and b[0] == 0):
                    act.wait_ge(cw_made, nth(b, 1, 0))
                fn(relu_ln1[:, 0:UB], tp[:, 0:UB], ACT.Copy).then_inc(ln1_copied, 1)

            def ffn(p, c):
                if c == RELU:
                    act.wait_ge(agg_done, nth(p, 1, 1))
                    fn(relu_ln1[:, 0:UB], agg[p[0] % 2][:, 0:UB], ACT.Relu, bias=buser[:, 0:1]).then_inc(relu_made, 1)
                if c == LN2_T:
                    act.wait_ge(ln2_rstd, nth(p, 1, 1))
                    act.wait_ge(ln1_transposed, nth(p, 1, 1))
                    for s in range(SUBS):
                        last = fn(lntok[0:TS, s * D:(s + 1) * D], tp[0:TS, s * D:(s + 1) * D], ACT.Identity,
                                  scale=rs2[0:TS, 1, s:s + 1], bias=rs2[0:TS, 2, s:s + 1])
                    last.then_inc(ln2_normed, 1)
                if c == Z_SPLIT:
                    act.wait_ge(ln2_transposed, nth(p, 1, 1))
                    fn(z_hi[:, :], tp[:, 0:UB], ACT.Copy).then_inc(z_hi_made, 1)
                if c == CW_T + 2:
                    act.wait_ge(cw_transposed, nth(p, 1, 1))
                    fn(cwt[:, :], small[0:2 * E, 0:UB], ACT.Copy).then_inc(cw_ready, 1)
                for e in range(E):
                    if c == SPLIT_AT[e]:
                        act.wait_ge(gw_made, nth(p, E, e + 1))
                        if not (p[1] is None and p[0] == 0 and e == 0):
                            act.wait_ge(w2_done, nth(p, E, e))
                        fn(gwh[:, :], gw[:, 0:HALVES * UB], ACT.Copy).then_inc(gwhi_made, 1)
                    if c == GELU_AT[e]:
                        act.wait_ge(hid_ready, nth(p, E, e + 1))
                        if not (p[1] is None and p[0] == 0 and e < 2):
                            act.wait_ge(gw_made, nth(p, E, e - 1))
                        for h in range(HALVES):
                            k = e * HALVES + h
                            last = fn(g[:, e % 2, h * UB:(h + 1) * UB], hid[h][:, 0:UB], ACT.Gelu,
                                      bias=b1s[:, k:k + 1])
                        last.then_inc(gelu_done, 1)

            def iteration(b):
                for c in range(CHUNKS):
                    hi_chunk(b, c)
                    if not (b[1] is None and b[0] < 2):
                        ffn((b[0] - 2, b[1]), CHUNKS + c)
                    ffn((b[0] - 1, b[1]), c)
                    if c == 16:
                        tail_round(b)
                    if c == LN1_T + 2:
                        ln1_copy(b)

            def h_round(c):
                act.wait_ge(h_biased, c + 1)
                fn(h_hi[:, c * KC * D:(c + 1) * KC * D], lntok[:, (c % 2) * KC * D:(c % 2 + 1) * KC * D],
                   ACT.Copy).then_inc(h_hi_made, 1)

            h_round(0)
            h_round(1)
            for c in range(CHUNKS):
                hi_chunk((0, None), c)
                if c + 2 < CHUNKS:
                    h_round(c + 2)
                if c + 2 == CHUNKS:
                    act.wait_ge(h_biased, CHUNKS + 1)
                    fn(h_tail[:, :], xt[0:TAILP, 1, 0:D], ACT.Copy).then_inc(h_hi_made, 1)
                for i, (hi, _, _, rows, o) in enumerate(pieces):
                    if c == PIECE_AT[i]:
                        act.wait_ge(piece_loaded, 16 * (i + 1))
                        fn(hi[:, o:o + widths[i]], gw[0:rows, 0:widths[i]], ACT.Copy).then_inc(piece_hi, 1)
                if c == 16:
                    tail_round((0, None))
            ln1_copy((0, None))
            iteration((1, None))
            with act.Fori(0, (BLOCKS - 2) // 2) as t:
                iteration((2, t))
                iteration((3, t))
            for c in range(CHUNKS):
                ffn((BLOCKS - 2, None), CHUNKS + c)
                ffn((BLOCKS - 1, None), c)
            for c in range(CHUNKS, ENDS):
                ffn((BLOCKS - 1, None), c)

        @block.vector
        def _(dve):
            tt = nc.vector.tensor_tensor

            def lo_chunk(b, c):
                n = CHUNKS * b[0] + c
                dve.wait_ge(hi_made, nth(b, CHUNKS, c + 1))
                tt(a_lo[:, c % PARTS, :], raw[:, n % RAW, :], a_hi[:, c % PARTS, :].bitcast(F32),
                   ALU.subtract).then_inc(lo_made, 1)

            def tail_rest(b):
                dve.wait_ge(tail_hi, nth(b, 1, 1))
                m = tail_parts[32:64, :]
                tt(m, tail_raw[32:64, :], m.bitcast(F32), ALU.subtract).then_inc(tail_split, 1)

            def ln1(b, c):
                if c == LN1_BN:
                    if not (b[1] is None and b[0] == 0):
                        dve.wait_ge(ln1_normed, nth(b, 1, 0))
                    dve.wait_ge(xtok_loaded, nth(b, 16, 16))
                    for s in range(SUBS):
                        last = nc.vector.bn_stats(bn6[0:TS, s, :], xtok[0:TS, s * D:(s + 1) * D])
                    last.then_inc(ln1_stats, 1)

            def out_step(p):
                if not (p[1] is None and p[0] == 0):
                    dve.wait_ge(out_stored, nth(p, 16, 0))
                dve.wait_ge(w2_done, nth(p, E, E))
                tt(y_out[:, 0:UB], y[:, 0:UB], xt[:, p[0] % 2, :], ALU.add).then_inc(out_made, 1)

            GS = 10

            def ffn(p, c):
                sub_e = [TS, SUBS, E]
                if c == OUT_AT:
                    out_step(p)
                if c == LN2_BN:
                    dve.wait_ge(x1_transposed, nth(p, 1, 1))
                    for s in range(SUBS):
                        last = nc.vector.bn_stats(bn6b[0:TS, s, :], tp[0:TS, s * D:(s + 1) * D])
                    last.then_inc(ln2_stats, 1)
                if c == Z_SPLIT:
                    dve.wait_ge(z_hi_made, nth(p, 1, 1))
                    tt(z_lo[:, :], tp[:, 0:UB], z_hi[:, :].bitcast(F32), ALU.subtract).then_inc(z_split, 1)
                if c == GATE + 2:
                    dve.wait_ge(gate_done, nth(p, 1, 1))
                    tt(lg[0:TS, :, :], small[0:TS, 0:SUBS * E].rearrange("p (s e) -> p s e", e=E),
                       gateb[0:TS, :].rearrange("p (s e) -> p s e", e=E), ALU.add).then_inc(gate_step, 1)
                    dve.wait_ge(gate_step, nth(p, GS, 1))
                    nc.vector.reduce_max(col[0:TS, 0, :], lg[0:TS, :, :], AX.X).then_inc(gate_step, 1)
                if c == GATE + 3:
                    dve.wait_ge(gate_step, nth(p, GS, 2))
                    tt(zz3[0:TS, :, :], lg[0:TS, :, :],
                       col[0:TS, 0, :].unsqueeze(2).to_broadcast(sub_e), ALU.subtract).then_inc(z_made, 1)
                if c == CW_STEP:
                    dve.wait_ge(ez_made, nth(p, 1, 1))
                    nc.vector.reduce_sum(col[0:TS, 1, :], ez[0:TS, :, :], AX.X).then_inc(gate_step, 1)
                    dve.wait_ge(gate_step, nth(p, GS, 3))
                    nc.vector.reciprocal(col[0:TS, 2, :], col[0:TS, 1, :]).then_inc(gate_step, 1)
                if c == CW_STEP + 1:
                    dve.wait_ge(gate_step, nth(p, GS, 4))
                    tt(pr[0:TS, :, :], ez[0:TS, :, :], col[0:TS, 2, :].unsqueeze(2).to_broadcast(sub_e),
                       ALU.mult).then_inc(gate_step, 1)
                    dve.wait_ge(gate_step, nth(p, GS, 5))
                    wide = [TS, SUBS, E, E]
                    other = pr[0:TS, :, :].unsqueeze(2).to_broadcast(wide)
                    own = pr[0:TS, :, :].unsqueeze(3).to_broadcast(wide)
                    tt(above[0:TS, :, :, :], other, own, ALU.is_gt)
                    tt(equal[0:TS, :, :, :], other, own, ALU.is_equal).then_inc(gate_step, 1)
                if c == CW_STEP + 2:
                    dve.wait_ge(gate_step, nth(p, GS, 6))
                    tt(equal[0:TS, :, :, :], equal[0:TS, :, :, :],
                       tri[0:TS, :, :].unsqueeze(1).to_broadcast([TS, SUBS, E, E]), ALU.mult)\
                        .then_inc(gate_step, 1)
                    dve.wait_ge(gate_step, nth(p, GS, 7))
                    tt(above[0:TS, :, :, :], above[0:TS, :, :, :], equal[0:TS, :, :, :], ALU.add)\
                        .then_inc(gate_step, 1)
                if c == CW_STEP + 3:
                    dve.wait_ge(gate_step, nth(p, GS, 8))
                    nc.vector.reduce_sum(rank[0:TS, :, :], above[0:TS, :, :, :], AX.X).then_inc(gate_step, 1)
                    dve.wait_ge(gate_step, nth(p, GS, 9))
                    nc.vector.scalar_tensor_tensor(out=cw[0:TS, :, :], in0=rank[0:TS, :, :], scalar=2.0,
                                                   in1=pr[0:TS, :, :], op0=ALU.is_lt, op1=ALU.mult)\
                        .then_inc(gate_step, 1)
                if c == CW_STEP + 4:
                    dve.wait_ge(gate_step, nth(p, GS, 10))
                    nc.vector.tensor_copy(cwr[0:TS, :, 0:E], cw[0:TS, :, :]).then_inc(cwhi_made, 1)
                    dve.wait_ge(cwhi_made, nth(p, 1, 1))
                    tt(cwr[0:TS, :, E:2 * E], cw[0:TS, :, :], cwr[0:TS, :, 0:E].bitcast(F32),
                       ALU.subtract).then_inc(cw_made, 1)
                for e in range(E):
                    if c == SPLIT_AT[e]:
                        dve.wait_ge(gwhi_made, nth(p, E, e + 1))
                        tt(gwl[:, :], gw[:, 0:HALVES * UB], gwh[:, :].bitcast(F32), ALU.subtract)\
                            .then_inc(gw_split, 1)
                    if c == GW_AT[e]:
                        dve.wait_ge(gelu_done, nth(p, E, e + 1))
                        dve.wait_ge(wbc_ready, nth(p, E, e + 1))
                        if not (p[1] is None and p[0] == 0 and e == 0):
                            dve.wait_ge(gw_split, nth(p, E, e))
                        tt(gw[:, 0:HALVES * UB].rearrange("p (h n) -> p h n", h=HALVES),
                           g[:, e % 2, :].rearrange("p (h n) -> p h n", h=HALVES),
                           wbc[:, 0:UB].unsqueeze(1).to_broadcast([P, HALVES, UB]), ALU.mult)\
                            .then_inc(gw_made, 1)

            def iteration(b):
                for c in range(CHUNKS):
                    lo_chunk(b, c)
                    if not (b[1] is None and b[0] < 2):
                        ffn((b[0] - 2, b[1]), CHUNKS + c)
                    ffn((b[0] - 1, b[1]), c)
                    if c == 17:
                        tail_rest(b)
                    ln1(b, c)

            def h_bias(c):
                hf = lntok[:, (c % 2) * KC * D:(c % 2 + 1) * KC * D]
                if c == 0:
                    dve.wait_ge(item_loaded, 16 * 2)
                dve.wait_ge(h_prod, c + 1)
                if c >= 2:
                    dve.wait_ge(h_made, c - 1)
                tt(hf, hid[c % 2][:, 0:KC * D], bitem[:, :], ALU.add).then_inc(h_biased, 1)

            def h_rest(c):
                hf = lntok[:, (c % 2) * KC * D:(c % 2 + 1) * KC * D]
                cols = slice(c * KC * D, (c + 1) * KC * D)
                dve.wait_ge(h_hi_made, c + 1)
                tt(h_lo[:, cols], hf, h_hi[:, cols].bitcast(F32), ALU.subtract).then_inc(h_made, 1)

            h_bias(0)
            h_bias(1)
            h_rest(0)
            h_rest(1)
            for c in range(CHUNKS):
                lo_chunk((0, None), c)
                if c + 2 < CHUNKS:
                    h_bias(c + 2)
                    h_rest(c + 2)
                if c + 2 == CHUNKS:
                    dve.wait_ge(h_prod, CHUNKS + 1)
                    tt(xt[0:TAILP, 1, 0:D], wbc[0:TAILP, 0:D], bitem[0:TAILP, 0:D], ALU.add).then_inc(h_biased, 1)
                    dve.wait_ge(h_hi_made, CHUNKS + 1)
                    m = h_tail[64:TAILP, :]
                    tt(m, xt[64:TAILP, 1, 0:D], m.bitcast(F32), ALU.subtract).then_inc(h_made, 1)
                for i, (hi, lo, _, rows, o) in enumerate(pieces):
                    if c == PIECE_AT[i]:
                        dve.wait_ge(piece_hi, i + 1)
                        if lo is None:
                            dve.engine_nop().then_inc(piece_split, 1)
                        else:
                            tt(lo[:, o:o + widths[i]], gw[0:rows, 0:widths[i]],
                               hi[:, o:o + widths[i]].bitcast(F32), ALU.subtract).then_inc(piece_split, 1)
                if c == 17:
                    tail_rest((0, None))
                ln1((0, None), c)
            iteration((1, None))
            with dve.Fori(0, (BLOCKS - 2) // 2) as t:
                iteration((2, t))
                iteration((3, t))
            for c in range(CHUNKS):
                ffn((BLOCKS - 2, None), CHUNKS + c)
                ffn((BLOCKS - 1, None), c)
            for c in range(CHUNKS, ENDS):
                ffn((BLOCKS - 1, None), c)

        @block.gpsimd
        def _(pool):
            gp = nc.gpsimd

            def rstd(bn, rs, step, b):
                n = 6
                row = [rs[0:TS, i, :] for i in range(6)]
                inv_n, quarter, eps, mhalf = (consts[0:TS, i, :] for i in range(4))
                tt = gp.tensor_tensor
                even, odd = bn[0:TS, :, 1], bn[0:TS, :, 4]
                tt(row[0], even, odd, ALU.add)
                tt(row[3], even, odd, ALU.subtract)
                tt(row[4], bn[0:TS, :, 2], bn[0:TS, :, 5], ALU.add).then_inc(step, 1)
                pool.wait_ge(step, nth(b, n, 1))
                tt(row[3], row[3], row[3], ALU.mult)
                tt(row[4], row[4], inv_n, ALU.mult).then_inc(step, 1)
                pool.wait_ge(step, nth(b, n, 2))
                tt(row[3], row[3], quarter, ALU.mult)
                tt(row[4], row[4], eps, ALU.add).then_inc(step, 1)
                pool.wait_ge(step, nth(b, n, 3))
                tt(row[5], row[3], row[4], ALU.add).then_inc(step, 1)
                pool.wait_ge(step, nth(b, n, 4))
                tt(row[1], row[5], mhalf, ALU.pow).then_inc(step, 1)
                pool.wait_ge(step, nth(b, n, 5))
                tt(row[3], row[1], row[0], ALU.mult).then_inc(step, 1)
                pool.wait_ge(step, nth(b, n, 6))
                return tt(row[2], row[3], mhalf, ALU.mult)

            def ln1(b):
                pool.wait_ge(ln1_stats, nth(b, 1, 1))
                if b[1] is None and b[0] == 0:
                    pool.wait_ge(h_made, CHUNKS)
                else:
                    pool.wait_ge(ln2_transposed, nth(b, 1, 0))
                rstd(bn6, rs1, pool_step1, b).then_inc(ln1_rstd, 1)
                pool.wait_ge(ln1_rstd, nth(b, 1, 1))
                x3 = xtok[0:TS, :].rearrange("p (s d) -> p s d", d=D)
                l3 = lntok[0:TS, :].rearrange("p (s d) -> p s d", d=D)
                gp.tensor_tensor(l3, x3, rs1[0:TS, 1, :].unsqueeze(2).to_broadcast([TS, SUBS, D]), ALU.mult)\
                    .then_inc(ln1_scaled, 1)
                pool.wait_ge(ln1_scaled, nth(b, 1, 1))
                gp.tensor_tensor(l3, l3, rs1[0:TS, 2, :].unsqueeze(2).to_broadcast([TS, SUBS, D]), ALU.add)\
                    .then_inc(ln1_normed, 1)

            def ffn(p):
                xb = xt[:, p[0] % 2, :]
                pool.wait_ge(relu_made, nth(p, 1, 1))
                pool.wait_ge(xt_loaded, nth(p, 16, 16))
                gp.tensor_tensor(xb, xb, relu_ln1[:, 0:UB], ALU.add).then_inc(x1_made, 1)
                pool.wait_ge(ln2_stats, nth(p, 1, 1))
                rstd(bn6b, rs2, pool_step2, p).then_inc(ln2_rstd, 1)
                pool.wait_ge(z_made, nth(p, 1, 1))
                gp.tensor_tensor(bitem[0:TS, 2 * SUBS * E:3 * SUBS * E], ebase[0:TS, :], zz[0:TS, :],
                                 ALU.pow).then_inc(ez_made, 1)

            for i, value in enumerate((1.0 / D, 0.25, EPS, -0.5)):
                gp.memset(consts[:, i, :], value).then_inc(consts_set, 1)
            gp.memset(ebase[:, :], 2.718281828459045).then_inc(consts_set, 1)
            pool.wait_ge(consts_set, 5)
            ln1((0, None))
            ffn((0, None))
            ln1((1, None))
            with pool.Fori(0, (BLOCKS - 2) // 2) as t:
                ffn((1, t))
                ln1((2, t))
                ffn((2, t))
                ln1((3, t))
            ffn((BLOCKS - 1, None))



def kernel(**inputs):
    import numpy as np
    import concourse.bacc as bacc
    from concourse.bass_utils import run_bass_kernel_spmd as run

    def f(name):
        return np.asarray(inputs[name])

    cut = KT * P
    adj = f("adj")
    a = adj[:, :cut].reshape(BLOCKS, UB, CHUNKS, KC, P).transpose(2, 0, 4, 3, 1)
    a = np.ascontiguousarray(a).reshape(CHUNKS, BLOCKS, P, KC * UB)
    at = adj[:, cut:].reshape(BLOCKS, UB, TAIL).transpose(0, 2, 1)
    tail = np.zeros((BLOCKS, TAILP, UB), np.float32)
    x = f("x")
    xtok = np.zeros((BLOCKS, P, SUBS, D), np.float32)
    xtok[:, :TS] = x.reshape(BLOCKS, SUBS, TS, D).transpose(0, 2, 1, 3)
    feat = f("L0_gnn_item_feat")
    feat_tail = np.zeros((P, TAILP), np.float32)
    for r in (0, 32, 64):
        tail[:, r:r + TAIL] = at
        feat_tail[:, r:r + TAIL] = feat[cut:].T
    n_feat = CHUNKS // FEAT
    sel = np.zeros((2 * E, E, P), np.float32)
    for e in range(E):
        sel[[e, E + e], e] = 1.0
    tri = np.tile((np.arange(E)[None, :] < np.arange(E)[:, None]).astype(np.float32), (P, 1, 1))
    arrays = {
        "adj": a,
        "adj_tail": tail,
        "x_tok": xtok.reshape(BLOCKS, P, SUBS * D),
        "x_t": x.reshape(BLOCKS, UB, D).transpose(0, 2, 1),
        "feat_t": feat[:cut].reshape(n_feat, cut // n_feat, D).transpose(0, 2, 1),
        "feat_tail": feat_tail,
        "wi_t": f("L0_gnn_W_item").T,
        "b_item": np.tile(f("L0_gnn_b_item"), (P, KC)),
        "wu_t": f("L0_gnn_W_user").T,
        "b_user": f("L0_gnn_b_user").reshape(D, 1),
        "gate_w": f("L0_ffn_gate_w"),
        "gate_b": np.tile(f("L0_ffn_gate_b"), (P, SUBS)),
        "w1": f("L0_ffn_W1").transpose(1, 0, 2).reshape(D, E * HID),
        "b1": f("L0_ffn_b1").reshape(E * HALVES, P).T,
        "w2": f("L0_ffn_W2").reshape(E, HALVES, P, D).transpose(2, 0, 1, 3).reshape(P, E * HALVES * D),
        "b2": np.tile(f("L0_ffn_b2"), (2, 1)),
        "ident": np.eye(P, dtype=np.float32),
        "sel": sel.reshape(2 * E, E * P),
        "tri": tri,
    }
    arrays = {k: np.ascontiguousarray(v) for k, v in arrays.items()}
    nc = bacc.Bacc("TRN2", target_bir_lowering=False, num_devices=1)
    args = [nc.dram_tensor(k, v.shape, F32, kind="ExternalInput").ap() for k, v in arrays.items()]
    out = nc.dram_tensor("out", (BLOCKS, D, UB), F32, kind="ExternalOutput").ap()
    build(nc, *args, out)
    r = run(nc, [arrays], core_ids=[0])
    return np.ascontiguousarray(r.results[0]["out"].transpose(0, 2, 1)).reshape(N_USER, D)
```

```python
import concourse.bass as bass
from concourse import mybir
from concourse.alu_op_type import AluOpType as ALU
from contextlib import ExitStack

F32 = mybir.dt.float32
F32R = mybir.dt.float32r
ACT = mybir.ActivationFunctionType
AX = mybir.AxisListType

P = 128
N_USER, N_ITEM, D, HID, E = 10000, 10000, 128, 256, 8
BLOCKS = 20
UB = N_USER // BLOCKS
SUBS = 4
TS = UB // SUBS
KT = N_ITEM // P
TAIL = N_ITEM - KT * P
KC = 2
CHUNKS = KT // KC
RAW, PARTS = 6, 3
TAILP = 96
HALVES = HID // P
EPS = 1e-5
WPIECE = 1024
FEAT = 3

RELU = 3
X1_T = 6
LN2_BN = 9
LN2_NORM = 12
LN2_T = 11
Z_SPLIT = 13
GATE = 13
GATE_STEP = 14
CW_STEP = 19
CW_T = 23
CW_COPY = 27
WBC_AT = [26, 29, 32, 35, 38, 42, 45, 48]
W1_AT = [17, 20, 29, 32, 35, 39, 42, 45]
GELU_AT = [20, 23, 32, 35, 38, 42, 45, 48]
GW_AT = [29, 32, 35, 39, 41, 45, 48, 51]
W2_AT = [31, 34, 37, 40, 43, 47, 50, 53]
SPLIT_AT = [30, 34, 37, 40, 43, 47, 50, 53]
OUT_AT = 55
TAIL_AT = 14
LN1_BN = 18
LN1_T = 26
LN1_COPY = 29
LAST_W1 = 15
LAG = 3
EARLY = RAW
assert OUT_AT < 2 * CHUNKS
assert KT % KC == 0 and UB % SUBS == 0 and (2 * CHUNKS) % RAW == 0 and CHUNKS % PARTS == 0


def nth(b, per_block, k):
    base, t = b
    v = per_block * base + k
    return v if t is None else v + 2 * per_block * t


def build(nc, adj, adj_tail, x_tok, x_t, feat_t, feat_tail, wi_t, b_item, wu_t, b_user,
          gate_w, gate_b, w1, b1, w2, b2, ident_d, sel_d, tri_d, out):
    ctx = ExitStack()
    with ctx:
        def sb(name, shape, dt=F32):
            return ctx.enter_context(nc.sbuf_tensor("s_" + name, shape, dt))

        def sem(name):
            return ctx.enter_context(nc.semaphore(name))

        raw = sb("raw", [P, RAW, KC * UB])
        a_hi = sb("a_hi", [P, PARTS, KC * UB], F32R)
        a_lo = sb("a_lo", [P, PARTS, KC * UB], F32R)
        tail_raw = sb("tail_raw", [TAILP, UB])
        tail_parts = sb("tail_parts", [TAILP, UB], F32R)
        h_hi = sb("h_hi", [P, KT * D], F32R)
        h_lo = sb("h_lo", [P, KT * D], F32R)
        h_tail = sb("h_tail", [TAILP, D], F32R)
        w1_hi = sb("w1_hi", [P, E * HID], F32R)
        w1_lo = sb("w1_lo", [P, E * HID], F32R)
        w2_hi = sb("w2_hi", [P, E * HALVES * D], F32R)
        w2_lo = sb("w2_lo", [P, E * HALVES * D], F32R)
        b2_hi = sb("b2_hi", [2 * E, D], F32R)
        b2_lo = sb("b2_lo", [2 * E, D], F32R)
        sel = sb("sel", [2 * E, E * P], F32R)
        gate_parts = sb("gate_parts", [P, 2 * E], F32R)
        gatew = sb("gatew", [P, E])
        gateb = sb("gateb", [P, SUBS * E])
        wi = sb("wi", [P, D])
        wu = sb("wu", [P, D])
        bitem = sb("bitem", [P, KC * D])
        buser = sb("buser", [P, 1])
        b1s = sb("b1s", [P, E * HALVES])
        ident = sb("ident", [P, P])
        tri = sb("tri", [P, E, E])
        xtok = sb("xtok", [P, SUBS * D])
        xt = sb("xt", [P, 2, UB])
        relu_ln1 = sb("relu_ln1", [P, 2 * SUBS * E * E])
        lntok = sb("lntok", [P, SUBS * D])
        z_hi = sb("z_hi", [P, UB], F32R)
        z_lo = sb("z_lo", [P, UB], F32R)
        g = sb("g", [P, 2, HALVES * UB])
        gw = sb("gw", [P, WPIECE])
        gwh = sb("gwh", [P, HALVES * UB], F32R)
        gwl = sb("gwl", [P, HALVES * UB], F32R)
        cwt = sb("cwt", [2 * E, UB], F32R)
        y_out = sb("y_out", [P, UB])
        bn6 = sb("bn6", [P, SUBS, 6])
        bn6b = sb("bn6b", [P, SUBS, 6])
        rs1 = sb("rs1", [P, 6, SUBS])
        rs2 = sb("rs2", [P, 6, SUBS])
        consts = sb("consts", [P, 4, SUBS])
        ebase = sb("ebase", [P, SUBS * E])
        col = sb("col", [P, 4, SUBS])
        lg, zz3, ez, pr, rank, cw = (bitem[:, i * SUBS * E:(i + 1) * SUBS * E].rearrange("p (s e) -> p s e", e=E)
                                     for i in range(6))
        zz = bitem[:, SUBS * E:2 * SUBS * E]
        above = relu_ln1[:, 0:SUBS * E * E].rearrange("p (s e f) -> p s e f", e=E, f=E)
        equal = relu_ln1[:, SUBS * E * E:2 * SUBS * E * E].rearrange("p (s e f) -> p s e f", e=E, f=E)
        cwr = sb("cwr", [P, SUBS, 2 * E], F32R)

        def bank(name):
            return ctx.enter_context(nc.psum_tensor("p_" + name, [P, 512], F32))

        agg = [bank("agg0"), bank("agg1")]
        hid = [bank("hid0"), bank("hid1")]
        wbc, y, tp, small = bank("wbc"), bank("y"), bank("tp"), bank("small")

        raw_loaded = [sem(f"raw_loaded{i}") for i in range(RAW)]
        item_loaded, weights_loaded, piece_loaded = sem("item_loaded"), sem("weights_loaded"), sem("piece_loaded")
        feat_loaded = [sem("feat_loaded0"), sem("feat_loaded1")]
        xt_loaded, xtok_loaded, tail_loaded, y_out_moved = (
            sem("xt_loaded"), sem("xtok_loaded"), sem("tail_loaded"), sem("y_out_moved"))
        hi_made, lo_made, chunk_used = sem("hi_made"), sem("lo_made"), sem("chunk_used")
        h_prod, h_biased, h_hi_made, h_made = sem("h_prod"), sem("h_biased"), sem("h_hi_made"), sem("h_made")
        piece_hi, piece_split = sem("piece_hi"), sem("piece_split")
        tail_hi, tail_split = sem("tail_hi"), sem("tail_split")
        consts_set = sem("consts_set")
        agg_done, relu_made, x1_made = sem("agg_done"), sem("relu_made"), sem("x1_made")
        x1_transposed, ln2_stats, ln2_rstd, ln2_normed = (
            sem("x1_transposed"), sem("ln2_stats"), sem("ln2_rstd"), sem("ln2_normed"))
        ln2_transposed, z_hi_made, z_split = sem("ln2_transposed"), sem("z_hi_made"), sem("z_split")
        ln1_stats, ln1_normed, ln1_transposed, ln1_copied = (
            sem("ln1_stats"), sem("ln1_normed"), sem("ln1_transposed"), sem("ln1_copied"))
        cwhi_made, ln1_rstd, ln1_scaled = sem("cwhi_made"), sem("ln1_rstd"), sem("ln1_scaled")
        pool_step1, pool_step2 = sem("pool_step1"), sem("pool_step2")
        gate_done, z_made, ez_made, gate_step, cw_made, cw_transposed, cw_ready = (
            sem("gate_done"), sem("z_made"), sem("ez_made"), sem("gate_step"), sem("cw_made"),
            sem("cw_transposed"), sem("cw_ready"))
        hid_ready, gelu_done, wbc_ready, gw_made, gwhi_made, gw_split, w2_done, out_made = (
            sem("hid_ready"), sem("gelu_done"), sem("wbc_ready"), sem("gw_made"), sem("gwhi_made"),
            sem("gw_split"), sem("w2_done"), sem("out_made"))

        NW = 7
        pieces = [(w1_hi, w1_lo, w1, P, 0), (w1_hi, w1_lo, w1, P, WPIECE),
                  (w2_hi, w2_lo, w2, P, 0), (w2_hi, w2_lo, w2, P, WPIECE),
                  (sel, None, sel_d, 2 * E, 0), (b2_hi, b2_lo, b2, 2 * E, 0),
                  (gate_parts[:, 0:E], gate_parts[:, E:2 * E], gate_w, P, 0)]
        widths = [WPIECE] * 4 + [E * P, D, E]
        PIECE_AT = [4 + 5 * i for i in range(len(pieces))]
        gstage = g[:, :, :].rearrange("p a n -> p (a n)")
        FW = FEAT * KC * P

        def feat_at(c):
            o = (c // FEAT % 2) * FW + c % FEAT * KC * P
            return gstage[:, o:o + KC * P]

        block = ctx.enter_context(nc.Block())

        @block.sync
        def _(sp):
            def load_raw(b, c):
                s = (CHUNKS * b[0] + c) % RAW
                if not (b[1] is None and CHUNKS * b[0] + c < RAW):
                    sp.wait_ge(lo_made, nth(b, CHUNKS, c - RAW + 1))
                row = b[0] if b[1] is None else b[0] + 2 * b[1]
                src = adj[c, row] if b[1] is None else adj[c, bass.ds(row, 1)].rearrange("a p n -> (a p) n")
                sp.dma_start(raw[:, s, :], src).then_inc(raw_loaded[s], 16)

            def load_block(b):
                start = b[1] is None
                row = b[0] if start else b[0] + 2 * b[1]

                def of(d):
                    return d[row] if start else d[bass.ds(row, 1)].rearrange("a p n -> (a p) n")
                if not (start and b[0] == 0):
                    sp.wait_ge(ln1_normed, nth(b, 1, 0))
                sp.dma_start(xtok[:, :], of(x_tok)).then_inc(xtok_loaded, 16)
                if not (start and b[0] == 0):
                    sp.wait_ge(tail_split, nth(b, 1, 0))
                sp.dma_start(tail_raw[:, :], of(adj_tail)).then_inc(tail_loaded, 16)

            def load_xt(b):
                start = b[1] is None
                row = b[0] if start else b[0] + 2 * b[1]
                if not (start and b[0] < 2):
                    sp.wait_ge(out_made, nth(b, 1, -1))
                if not (start and b[0] == 0):
                    sp.wait_ge(x1_made, nth(b, 1, 0))
                src = x_t[row] if start else x_t[bass.ds(row, 1)].rearrange("a p n -> (a p) n")
                sp.dma_start(xt[:, b[0] % 2, :], src).then_inc(xt_loaded, 16)

            def store_out(b):
                row = b[0] if b[1] is None else b[0] + 2 * b[1]
                dst = out[row] if b[1] is None else out[bass.ds(row, 1)].rearrange("a p n -> (a p) n")
                sp.wait_ge(out_made, nth(b, 1, 1))
                sp.dma_start(dst, y_out[:, 0:UB]).then_inc(y_out_moved, 16)

            def iteration(b):
                for c in range(CHUNKS):
                    load_raw(b, c)
                    if c == 8:
                        load_block(b)
                    if c == OUT_AT - CHUNKS + 7:
                        load_xt(b)
                        if not (b[1] is None and b[0] < 2):
                            store_out((b[0] - 2, b[1]))

            sp.dma_start(wi[:, :], wi_t).then_inc(item_loaded, 16)
            sp.dma_start(bitem[:, :], b_item).then_inc(item_loaded, 16)
            sp.dma_start(gstage[:, 0:FW], feat_t[0]).then_inc(feat_loaded[0], 16)
            late = [(wu, wu_t), (buser, b_user), (gatew, gate_w), (gateb, gate_b), (b1s, b1),
                    (ident, ident_d)]
            for c in range(CHUNKS):
                if c % FEAT == 2 and c + FEAT - 2 < CHUNKS:
                    k = c // FEAT + 1
                    if k >= 2:
                        sp.wait_ge(h_prod, (k - 1) * FEAT)
                    sp.dma_start(gstage[:, k % 2 * FW:(k % 2 + 1) * FW], feat_t[k])\
                        .then_inc(feat_loaded[k % 2], 16)
                load_raw((0, None), c)
                if c == 11:
                    for dst, src in late:
                        sp.dma_start(dst[:, :], src).then_inc(weights_loaded, 16)
                    sp.dma_start(tri[:, :, :], tri_d).then_inc(weights_loaded, 16)
                    sp.dma_start(y_out[:, 0:TAILP], feat_tail).then_inc(y_out_moved, 16)
                for i, (_, _, src, rows, o) in enumerate(pieces):
                    if c == PIECE_AT[i] + 2:
                        if i >= 1:
                            sp.wait_ge(piece_split, i)
                        sp.dma_start(gw[0:rows, 0:widths[i]], src[:, o:o + widths[i]]).then_inc(piece_loaded, 16)
                if c == 8:
                    load_block((0, None))
                if c == OUT_AT - CHUNKS + 7:
                    load_xt((0, None))
            iteration((1, None))
            with sp.Fori(0, (BLOCKS - 2) // 2) as t:
                iteration((2, t))
                iteration((3, t))
            store_out((BLOCKS - 2, None))
            store_out((BLOCKS - 1, None))
            sp.wait_ge(y_out_moved, 16 * (BLOCKS + 1))

        @block.tensor
        def _(pe):
            mm = nc.tensor.matmul

            def h_step(c):
                if c == 0:
                    pe.wait_ge(item_loaded, 16 * 2)
                pe.wait_ge(feat_loaded[c // FEAT % 2], 16 * (c // FEAT // 2 + 1))
                if c >= 2:
                    pe.wait_ge(h_biased, c - 1)
                f = feat_at(c)
                for j in range(KC):
                    last = mm(hid[c % 2][:, j * D:(j + 1) * D], f[:, j * P:(j + 1) * P], wi[:, :],
                              start=True, stop=True)
                last.then_inc(h_prod, 1)

            def h_tail_step():
                pe.wait_ge(weights_loaded, 16 * NW)
                pe.wait_ge(y_out_moved, 16)
                mm(wbc[0:TAILP, 0:D], y_out[:, 0:TAILP], wi[:, :], start=True, stop=True).then_inc(h_prod, 1)

            def agg_chunk(b, c):
                pe.wait_ge(lo_made, nth(b, CHUNKS, c + 1))
                s = c % PARTS
                for j in range(KC):
                    k = c * KC + j
                    hi = a_hi[:, s, j * UB:(j + 1) * UB]
                    lo = a_lo[:, s, j * UB:(j + 1) * UB]
                    hh, hl = h_hi[:, k * D:(k + 1) * D], h_lo[:, k * D:(k + 1) * D]
                    o = agg[b[0] % 2][:, 0:UB]
                    mm(o, hh, hi, start=(k == 0), stop=False)
                    mm(o, hh, lo, start=False, stop=False)
                    last = mm(o, hl, hi, start=False, stop=False)
                last.then_inc(chunk_used, 1)

            def agg_end(b):
                o = agg[b[0] % 2][:, 0:UB]
                pe.wait_ge(tail_split, nth(b, 1, 1))
                mm(o, h_tail[:, :], tail_parts[:, :], start=False, stop=False)
                pe.wait_ge(ln1_copied, nth(b, 1, 1))
                mm(o, wu[:, :], relu_ln1[:, 0:UB], start=False, stop=True).then_inc(agg_done, 1)

            def ln1_turn(b):
                pe.wait_ge(ln1_normed, nth(b, 1, 1))
                for s in range(SUBS):
                    last = nc.tensor.transpose(tp[:, s * TS:(s + 1) * TS],
                                               lntok[0:TS, s * D:(s + 1) * D], ident[0:TS, 0:TS])
                last.then_inc(ln1_transposed, 1)

            def ffn(p, c, experts=True):
                if c == X1_T:
                    pe.wait_ge(x1_made, nth(p, 1, 1))
                    pe.wait_ge(ln1_copied, nth(p, 1, 1))
                    for s in range(SUBS):
                        last = nc.tensor.transpose(tp[0:TS, s * D:(s + 1) * D],
                                                   xt[:, p[0] % 2, s * TS:(s + 1) * TS], ident[:, :])
                    last.then_inc(x1_transposed, 1)
                if c == LN2_T:
                    pe.wait_ge(ln2_normed, nth(p, 1, 1))
                    for s in range(SUBS):
                        last = nc.tensor.transpose(tp[:, s * TS:(s + 1) * TS],
                                                   lntok[0:TS, s * D:(s + 1) * D], ident[0:TS, 0:TS])
                    last.then_inc(ln2_transposed, 1)
                if c == GATE:
                    pe.wait_ge(z_split, nth(p, 1, 1))
                    if not (p[1] is None and p[0] == 0):
                        pe.wait_ge(cw_ready, nth(p, 1, 0))
                    for s in range(SUBS):
                        o = small[0:TS, s * 2 * E:(s + 1) * 2 * E]
                        zh, zl = z_hi[:, s * TS:(s + 1) * TS], z_lo[:, s * TS:(s + 1) * TS]
                        mm(o, zh, gate_parts[:, :], start=True, stop=False)
                        last = mm(o, zl, gate_parts[:, :], start=False, stop=True)
                    last.then_inc(gate_done, 1)
                if c == CW_T:
                    pe.wait_ge(cw_made, nth(p, 1, 1))
                    for s in range(SUBS):
                        last = nc.tensor.transpose(small[0:2 * E, s * TS:(s + 1) * TS],
                                                   cwr[0:TS, s, :].bitcast(F32), ident[0:TS, 0:TS])
                    last.then_inc(cw_transposed, 1)
                for e in range(E if experts else 0):
                    if c == W2_AT[e]:
                        if e == 0:
                            if not (p[1] is None and p[0] == 0):
                                pe.wait_ge(out_made, nth(p, 1, 0))
                            mm(y[:, 0:UB], b2_hi[:, :], cwt[:, :], start=True, stop=False)
                            mm(y[:, 0:UB], b2_lo[:, :], cwt[:, :], start=False, stop=False)
                        pe.wait_ge(gw_split, nth(p, E, e + 1))
                        for h in range(HALVES):
                            o = (e * HALVES + h) * D
                            gh, gl = gwh[:, h * UB:(h + 1) * UB], gwl[:, h * UB:(h + 1) * UB]
                            mm(y[:, 0:UB], w2_hi[:, o:o + D], gh, start=False, stop=False)
                            mm(y[:, 0:UB], w2_lo[:, o:o + D], gh, start=False, stop=False)
                            last = mm(y[:, 0:UB], w2_hi[:, o:o + D], gl, start=False,
                                      stop=(e == E - 1 and h == HALVES - 1))
                        last.then_inc(w2_done, 1)
                    if c == WBC_AT[e]:
                        if e == 0:
                            pe.wait_ge(cw_ready, nth(p, 1, 1))
                        if not (p[1] is None and p[0] == 0 and e == 0):
                            pe.wait_ge(gw_made, nth(p, E, e))
                        mm(wbc[:, 0:UB], sel[:, e * P:(e + 1) * P], cwt[:, :], start=True, stop=True)\
                            .then_inc(wbc_ready, 1)
                    if c == W1_AT[e]:
                        if not (p[1] is None and p[0] == 0 and e == 0):
                            pe.wait_ge(gelu_done, nth(p, E, e))
                        for h in range(HALVES):
                            o = e * HID + h * P
                            mm(hid[h][:, 0:UB], w1_hi[:, o:o + P], z_hi[:, :], start=True, stop=False)
                            mm(hid[h][:, 0:UB], w1_hi[:, o:o + P], z_lo[:, :], start=False, stop=False)
                            last = mm(hid[h][:, 0:UB], w1_lo[:, o:o + P], z_hi[:, :], start=False, stop=True)
                        last.then_inc(hid_ready, 1)

            def iteration(b):
                for c in range(CHUNKS):
                    agg_chunk(b, c)
                    if c == 0 and b == (1, None):
                        pe.wait_ge(h_made, CHUNKS + 1)
                        pe.wait_ge(piece_split, len(pieces))
                        agg_end(first)
                    if not (b[1] is None and b[0] < 2):
                        ffn((b[0] - 2, b[1]), CHUNKS + c)
                    ffn((b[0] - 1, b[1]), c)
                    if c == LN1_T:
                        pe.wait_ge(z_split, nth(b, 1, 0))
                        ln1_turn(b)
                agg_end(b)

            first = (0, None)
            h_step(0)
            h_step(1)
            h_step(2)
            for c in range(CHUNKS):
                if c + 3 < CHUNKS:
                    h_step(c + 3)
                if c + 3 == CHUNKS:
                    h_tail_step()
                pe.wait_ge(h_made, c + 1)
                agg_chunk(first, c)
            ln1_turn(first)
            iteration((1, None))
            with pe.Fori(0, (BLOCKS - 2) // 2) as t:
                iteration((2, t))
                iteration((3, t))
            def last_w1(e):
                pe.wait_ge(gelu_done, E * (BLOCKS - 1) + max(e - 1, 0))
                for h in range(HALVES):
                    o = e * HID + h * P
                    bank_h = (agg, hid)[e % 2][h]
                    mm(bank_h[:, 0:UB], w1_hi[:, o:o + P], z_hi[:, :], start=True, stop=False)
                    mm(bank_h[:, 0:UB], w1_lo[:, o:o + P], z_hi[:, :], start=False, stop=False)
                    last = mm(bank_h[:, 0:UB], w1_hi[:, o:o + P], z_lo[:, :], start=False, stop=True)
                last.then_inc(hid_ready, 1)

            for c in range(CHUNKS):
                ffn((BLOCKS - 2, None), CHUNKS + c)
                ffn((BLOCKS - 1, None), c, experts=False)
                e = c - LAST_W1
                if 0 <= e < EARLY:
                    last_w1(e)

            p = (BLOCKS - 1, None)
            for i in range(E + LAG):
                e = i + EARLY
                if e < E:
                    last_w1(e)
                e = i
                if e < E:
                    if e == 0:
                        pe.wait_ge(cw_ready, nth(p, 1, 1))
                    if e >= 2:
                        pe.wait_ge(gw_made, nth(p, E, e - 1))
                    mm((wbc, tp)[e % 2][:, 0:UB], sel[:, e * P:(e + 1) * P], cwt[:, :], start=True, stop=True)\
                        .then_inc(wbc_ready, 1)
                e = i - LAG
                if e >= 0:
                    if e == 0:
                        pe.wait_ge(out_made, nth(p, 1, 0))
                        mm(y[:, 0:UB], b2_hi[:, :], cwt[:, :], start=True, stop=False)
                        mm(y[:, 0:UB], b2_lo[:, :], cwt[:, :], start=False, stop=False)
                    pe.wait_ge(gw_split, nth(p, E, e + 1))
                    for h in range(HALVES):
                        o = (e * HALVES + h) * D
                        gh = a_hi[:, e % PARTS, h * UB:(h + 1) * UB]
                        gl = a_lo[:, e % PARTS, h * UB:(h + 1) * UB]
                        mm(y[:, 0:UB], w2_hi[:, o:o + D], gh, start=False, stop=False)
                        mm(y[:, 0:UB], w2_lo[:, o:o + D], gh, start=False, stop=False)
                        last = mm(y[:, 0:UB], w2_hi[:, o:o + D], gl, start=False,
                                  stop=(e == E - 1 and h == HALVES - 1))
                    last.then_inc(w2_done, 1)

        @block.scalar
        def _(act):
            fn = nc.scalar.activation

            def hi_chunk(b, c):
                n = CHUNKS * b[0] + c
                act.wait_ge(raw_loaded[n % RAW], 16 * (n // RAW + 1) if b[1] is None
                            else 16 * (n // RAW + 1) + 16 * (2 * CHUNKS // RAW) * b[1])
                if not (b[1] is None and n < PARTS):
                    act.wait_ge(chunk_used, nth(b, CHUNKS, c - PARTS + 1))
                fn(a_hi[:, c % PARTS, :], raw[:, n % RAW, :], ACT.Copy).then_inc(hi_made, 1)

            def tail_round(b):
                act.wait_ge(tail_loaded, nth(b, 16, 16))
                if not (b[1] is None and b[0] == 0):
                    act.wait_ge(agg_done, nth(b, 1, 0))
                fn(tail_parts[:, :], tail_raw[:, :], ACT.Copy).then_inc(tail_hi, 1)

            def ln1_copy(b):
                act.wait_ge(ln1_transposed, nth(b, 1, 1))
                if not (b[1] is None and b[0] == 0):
                    act.wait_ge(cw_made, nth(b, 1, 0))
                fn(relu_ln1[:, 0:UB], tp[:, 0:UB], ACT.Copy).then_inc(ln1_copied, 1)

            def ffn(p, c, experts=True):
                if c == RELU:
                    act.wait_ge(agg_done, nth(p, 1, 1))
                    fn(relu_ln1[:, 0:UB], agg[p[0] % 2][:, 0:UB], ACT.Relu, bias=buser[:, 0:1]).then_inc(relu_made, 1)
                if c == LN2_NORM:
                    act.wait_ge(ln2_rstd, nth(p, 1, 1))
                    act.wait_ge(ln1_transposed, nth(p, 1, 1))
                    for s in range(SUBS):
                        last = fn(lntok[0:TS, s * D:(s + 1) * D], tp[0:TS, s * D:(s + 1) * D], ACT.Identity,
                                  scale=rs2[0:TS, 1, s:s + 1], bias=rs2[0:TS, 2, s:s + 1])
                    last.then_inc(ln2_normed, 1)
                if c == Z_SPLIT:
                    act.wait_ge(ln2_transposed, nth(p, 1, 1))
                    fn(z_hi[:, :], tp[:, 0:UB], ACT.Copy).then_inc(z_hi_made, 1)
                if c == CW_COPY:
                    act.wait_ge(cw_transposed, nth(p, 1, 1))
                    fn(cwt[:, :], small[0:2 * E, 0:UB], ACT.Copy).then_inc(cw_ready, 1)
                for e in range(E if experts else 0):
                    if c == SPLIT_AT[e]:
                        act.wait_ge(gw_made, nth(p, E, e + 1))
                        if not (p[1] is None and p[0] == 0 and e == 0):
                            act.wait_ge(w2_done, nth(p, E, e))
                        fn(gwh[:, :], gw[:, 0:HALVES * UB], ACT.Copy).then_inc(gwhi_made, 1)
                    if c == GELU_AT[e]:
                        act.wait_ge(hid_ready, nth(p, E, e + 1))
                        if not (p[1] is None and p[0] == 0 and e < 2):
                            act.wait_ge(gw_made, nth(p, E, e - 1))
                        for h in range(HALVES):
                            k = e * HALVES + h
                            last = fn(g[:, e % 2, h * UB:(h + 1) * UB], hid[h][:, 0:UB], ACT.Gelu,
                                      bias=b1s[:, k:k + 1])
                        last.then_inc(gelu_done, 1)

            def iteration(b):
                for c in range(CHUNKS):
                    hi_chunk(b, c)
                    if c == 1 and b == (1, None):
                        ln1_copy((0, None))
                    if not (b[1] is None and b[0] < 2):
                        ffn((b[0] - 2, b[1]), CHUNKS + c)
                    ffn((b[0] - 1, b[1]), c)
                    if c == TAIL_AT:
                        tail_round(b)
                    if c == LN1_COPY:
                        ln1_copy(b)

            def h_round(c):
                act.wait_ge(h_biased, c + 1)
                fn(h_hi[:, c * KC * D:(c + 1) * KC * D], lntok[:, (c % 2) * KC * D:(c % 2 + 1) * KC * D],
                   ACT.Copy).then_inc(h_hi_made, 1)

            h_round(0)
            h_round(1)
            for c in range(CHUNKS):
                hi_chunk((0, None), c)
                if c + 2 < CHUNKS:
                    h_round(c + 2)
                if c + 2 == CHUNKS:
                    act.wait_ge(h_biased, CHUNKS + 1)
                    fn(h_tail[:, :], xt[0:TAILP, 1, 0:D], ACT.Copy).then_inc(h_hi_made, 1)
                for i, (hi, _, _, rows, o) in enumerate(pieces):
                    if c == PIECE_AT[i]:
                        act.wait_ge(piece_loaded, 16 * (i + 1))
                        fn(hi[:, o:o + widths[i]], gw[0:rows, 0:widths[i]], ACT.Copy).then_inc(piece_hi, 1)
                if c == TAIL_AT:
                    tail_round((0, None))
            iteration((1, None))
            with act.Fori(0, (BLOCKS - 2) // 2) as t:
                iteration((2, t))
                iteration((3, t))
            p = (BLOCKS - 1, None)

            def last_gelu(e):
                act.wait_ge(hid_ready, nth(p, E, e + 1))
                for h in range(HALVES):
                    k = e * HALVES + h
                    last = fn(raw[:, e % RAW, h * UB:(h + 1) * UB], (agg, hid)[e % 2][h][:, 0:UB],
                              ACT.Gelu, bias=b1s[:, k:k + 1])
                last.then_inc(gelu_done, 1)

            for c in range(CHUNKS):
                ffn((BLOCKS - 2, None), CHUNKS + c)
                e = c - LAST_W1 - 1
                if 0 <= e < EARLY:
                    if e == 0:
                        act.wait_ge(chunk_used, CHUNKS * BLOCKS)
                    last_gelu(e)
                ffn((BLOCKS - 1, None), c, experts=False)

            for e in range(E):
                act.wait_ge(gw_made, nth(p, E, e + 1))
                if e >= PARTS:
                    act.wait_ge(w2_done, nth(p, E, e - PARTS + 1))
                fn(a_hi[:, e % PARTS, :], raw[:, e % RAW, :], ACT.Copy).then_inc(gwhi_made, 1)
                if e >= 1 and e - 1 + EARLY < E:
                    act.wait_ge(gw_split, nth(p, E, e))
                    last_gelu(e - 1 + EARLY)

        @block.vector
        def _(dve):
            tt = nc.vector.tensor_tensor

            def lo_chunk(b, c):
                n = CHUNKS * b[0] + c
                dve.wait_ge(hi_made, nth(b, CHUNKS, c + 1))
                tt(a_lo[:, c % PARTS, :], raw[:, n % RAW, :], a_hi[:, c % PARTS, :].bitcast(F32),
                   ALU.subtract).then_inc(lo_made, 1)

            def tail_rest(b):
                dve.wait_ge(tail_hi, nth(b, 1, 1))
                m = tail_parts[32:64, :]
                tt(m, tail_raw[32:64, :], m.bitcast(F32), ALU.subtract).then_inc(tail_split, 1)

            def ln1(b, c):
                if c == LN1_BN:
                    if not (b[1] is None and b[0] == 0):
                        dve.wait_ge(ln1_normed, nth(b, 1, 0))
                    dve.wait_ge(xtok_loaded, nth(b, 16, 16))
                    for s in range(SUBS):
                        last = nc.vector.bn_stats(bn6[0:TS, s, :], xtok[0:TS, s * D:(s + 1) * D])
                    last.then_inc(ln1_stats, 1)

            def out_step(p):
                dve.wait_ge(y_out_moved, nth(p, 16, 16))
                dve.wait_ge(w2_done, nth(p, E, E))
                tt(y_out[:, 0:UB], y[:, 0:UB], xt[:, p[0] % 2, :], ALU.add).then_inc(out_made, 1)

            GS = 11

            def ffn(p, c, experts=True):
                sub_e = [TS, SUBS, E]
                if c == OUT_AT and experts:
                    out_step(p)
                if c == LN2_BN:
                    dve.wait_ge(x1_transposed, nth(p, 1, 1))
                    for s in range(SUBS):
                        last = nc.vector.bn_stats(bn6b[0:TS, s, :], tp[0:TS, s * D:(s + 1) * D])
                    last.then_inc(ln2_stats, 1)
                if c == Z_SPLIT:
                    dve.wait_ge(z_hi_made, nth(p, 1, 1))
                    tt(z_lo[:, :], tp[:, 0:UB], z_hi[:, :].bitcast(F32), ALU.subtract).then_inc(z_split, 1)
                if c == GATE_STEP:
                    dve.wait_ge(gate_done, nth(p, 1, 1))
                    both = small[0:TS, 0:SUBS * 2 * E].rearrange("p (s k e) -> p s k e", k=2, e=E)
                    tt(lg[0:TS, :, :], both[:, :, 0, :],
                       gateb[0:TS, :].rearrange("p (s e) -> p s e", e=E), ALU.add).then_inc(gate_step, 1)
                    dve.wait_ge(gate_step, nth(p, GS, 1))
                    tt(lg[0:TS, :, :], both[:, :, 1, :], lg[0:TS, :, :], ALU.add).then_inc(gate_step, 1)
                    dve.wait_ge(gate_step, nth(p, GS, 2))
                    nc.vector.reduce_max(col[0:TS, 0, :], lg[0:TS, :, :], AX.X).then_inc(gate_step, 1)
                if c == GATE_STEP + 1:
                    dve.wait_ge(gate_step, nth(p, GS, 3))
                    tt(zz3[0:TS, :, :], lg[0:TS, :, :],
                       col[0:TS, 0, :].unsqueeze(2).to_broadcast(sub_e), ALU.subtract).then_inc(z_made, 1)
                if c == CW_STEP:
                    dve.wait_ge(ez_made, nth(p, 1, 1))
                    nc.vector.reduce_sum(col[0:TS, 1, :], ez[0:TS, :, :], AX.X).then_inc(gate_step, 1)
                    dve.wait_ge(gate_step, nth(p, GS, 4))
                    nc.vector.reciprocal(col[0:TS, 2, :], col[0:TS, 1, :]).then_inc(gate_step, 1)
                if c == CW_STEP + 1:
                    dve.wait_ge(gate_step, nth(p, GS, 5))
                    tt(pr[0:TS, :, :], ez[0:TS, :, :], col[0:TS, 2, :].unsqueeze(2).to_broadcast(sub_e),
                       ALU.mult).then_inc(gate_step, 1)
                    dve.wait_ge(gate_step, nth(p, GS, 6))
                    wide = [TS, SUBS, E, E]
                    other = pr[0:TS, :, :].unsqueeze(2).to_broadcast(wide)
                    own = pr[0:TS, :, :].unsqueeze(3).to_broadcast(wide)
                    tt(above[0:TS, :, :, :], other, own, ALU.is_gt)
                    tt(equal[0:TS, :, :, :], other, own, ALU.is_equal).then_inc(gate_step, 1)
                if c == CW_STEP + 2:
                    dve.wait_ge(gate_step, nth(p, GS, 7))
                    tt(equal[0:TS, :, :, :], equal[0:TS, :, :, :],
                       tri[0:TS, :, :].unsqueeze(1).to_broadcast([TS, SUBS, E, E]), ALU.mult)\
                        .then_inc(gate_step, 1)
                    dve.wait_ge(gate_step, nth(p, GS, 8))
                    tt(above[0:TS, :, :, :], above[0:TS, :, :, :], equal[0:TS, :, :, :], ALU.add)\
                        .then_inc(gate_step, 1)
                if c == CW_STEP + 3:
                    dve.wait_ge(gate_step, nth(p, GS, 9))
                    nc.vector.reduce_sum(rank[0:TS, :, :], above[0:TS, :, :, :], AX.X).then_inc(gate_step, 1)
                    dve.wait_ge(gate_step, nth(p, GS, 10))
                    nc.vector.scalar_tensor_tensor(out=cw[0:TS, :, :], in0=rank[0:TS, :, :], scalar=2.0,
                                                   in1=pr[0:TS, :, :], op0=ALU.is_lt, op1=ALU.mult)\
                        .then_inc(gate_step, 1)
                if c == CW_STEP + 4:
                    dve.wait_ge(gate_step, nth(p, GS, 11))
                    nc.vector.tensor_copy(cwr[0:TS, :, 0:E], cw[0:TS, :, :]).then_inc(cwhi_made, 1)
                    dve.wait_ge(cwhi_made, nth(p, 1, 1))
                    tt(cwr[0:TS, :, E:2 * E], cw[0:TS, :, :], cwr[0:TS, :, 0:E].bitcast(F32),
                       ALU.subtract).then_inc(cw_made, 1)
                for e in range(E if experts else 0):
                    if c == SPLIT_AT[e]:
                        dve.wait_ge(gwhi_made, nth(p, E, e + 1))
                        tt(gwl[:, :], gw[:, 0:HALVES * UB], gwh[:, :].bitcast(F32), ALU.subtract)\
                            .then_inc(gw_split, 1)
                    if c == GW_AT[e]:
                        dve.wait_ge(gelu_done, nth(p, E, e + 1))
                        dve.wait_ge(wbc_ready, nth(p, E, e + 1))
                        if not (p[1] is None and p[0] == 0 and e == 0):
                            dve.wait_ge(gw_split, nth(p, E, e))
                        tt(gw[:, 0:HALVES * UB].rearrange("p (h n) -> p h n", h=HALVES),
                           g[:, e % 2, :].rearrange("p (h n) -> p h n", h=HALVES),
                           wbc[:, 0:UB].unsqueeze(1).to_broadcast([P, HALVES, UB]), ALU.mult)\
                            .then_inc(gw_made, 1)

            def iteration(b):
                for c in range(CHUNKS):
                    lo_chunk(b, c)
                    if not (b[1] is None and b[0] < 2):
                        ffn((b[0] - 2, b[1]), CHUNKS + c)
                    ffn((b[0] - 1, b[1]), c)
                    if c == TAIL_AT + 1:
                        tail_rest(b)
                    ln1(b, c)

            def h_bias(c):
                hf = lntok[:, (c % 2) * KC * D:(c % 2 + 1) * KC * D]
                if c == 0:
                    dve.wait_ge(item_loaded, 16 * 2)
                dve.wait_ge(h_prod, c + 1)
                if c >= 2:
                    dve.wait_ge(h_made, c - 1)
                tt(hf, hid[c % 2][:, 0:KC * D], bitem[:, :], ALU.add).then_inc(h_biased, 1)

            def h_rest(c):
                hf = lntok[:, (c % 2) * KC * D:(c % 2 + 1) * KC * D]
                cols = slice(c * KC * D, (c + 1) * KC * D)
                dve.wait_ge(h_hi_made, c + 1)
                tt(h_lo[:, cols], hf, h_hi[:, cols].bitcast(F32), ALU.subtract).then_inc(h_made, 1)

            h_bias(0)
            h_bias(1)
            h_rest(0)
            h_bias(2)
            h_rest(1)
            for c in range(CHUNKS):
                lo_chunk((0, None), c)
                if c + 2 < CHUNKS:
                    h_rest(c + 2)
                if c + 3 < CHUNKS:
                    h_bias(c + 3)
                if c + 3 == CHUNKS:
                    dve.wait_ge(h_prod, CHUNKS + 1)
                    tt(xt[0:TAILP, 1, 0:D], wbc[0:TAILP, 0:D], bitem[0:TAILP, 0:D], ALU.add).then_inc(h_biased, 1)
                if c + 2 == CHUNKS:
                    dve.wait_ge(h_hi_made, CHUNKS + 1)
                    m = h_tail[64:TAILP, :]
                    tt(m, xt[64:TAILP, 1, 0:D], m.bitcast(F32), ALU.subtract).then_inc(h_made, 1)
                for i, (hi, lo, _, rows, o) in enumerate(pieces):
                    if c == PIECE_AT[i] + 1:
                        dve.wait_ge(piece_hi, i + 1)
                        if lo is None:
                            dve.engine_nop().then_inc(piece_split, 1)
                        else:
                            tt(lo[:, o:o + widths[i]], gw[0:rows, 0:widths[i]],
                               hi[:, o:o + widths[i]].bitcast(F32), ALU.subtract).then_inc(piece_split, 1)
                if c == TAIL_AT + 1:
                    tail_rest((0, None))
                ln1((0, None), c)
            iteration((1, None))
            with dve.Fori(0, (BLOCKS - 2) // 2) as t:
                iteration((2, t))
                iteration((3, t))
            for c in range(CHUNKS):
                ffn((BLOCKS - 2, None), CHUNKS + c)
                ffn((BLOCKS - 1, None), c, experts=False)

            p = (BLOCKS - 1, None)
            for i in range(E + 1):
                e = i
                if e < E:
                    dve.wait_ge(gelu_done, nth(p, E, e + 1))
                    dve.wait_ge(wbc_ready, nth(p, E, e + 1))
                    gv = raw[:, e % RAW, :].rearrange("p (h n) -> p h n", h=HALVES)
                    tt(gv, gv, (wbc, tp)[e % 2][:, 0:UB].unsqueeze(1).to_broadcast([P, HALVES, UB]), ALU.mult)\
                        .then_inc(gw_made, 1)
                e = i - 1
                if e >= 0:
                    dve.wait_ge(gwhi_made, nth(p, E, e + 1))
                    tt(a_lo[:, e % PARTS, :], raw[:, e % RAW, :], a_hi[:, e % PARTS, :].bitcast(F32),
                       ALU.subtract).then_inc(gw_split, 1)
            out_step(p)

        @block.gpsimd
        def _(pool):
            gp = nc.gpsimd

            def rstd(bn, rs, step, b):
                n = 6
                row = [rs[0:TS, i, :] for i in range(6)]
                inv_n, quarter, eps, mhalf = (consts[0:TS, i, :] for i in range(4))
                tt = gp.tensor_tensor
                even, odd = bn[0:TS, :, 1], bn[0:TS, :, 4]
                tt(row[0], even, odd, ALU.add)
                tt(row[3], even, odd, ALU.subtract)
                tt(row[4], bn[0:TS, :, 2], bn[0:TS, :, 5], ALU.add).then_inc(step, 1)
                pool.wait_ge(step, nth(b, n, 1))
                tt(row[3], row[3], row[3], ALU.mult)
                tt(row[4], row[4], inv_n, ALU.mult).then_inc(step, 1)
                pool.wait_ge(step, nth(b, n, 2))
                tt(row[3], row[3], quarter, ALU.mult)
                tt(row[4], row[4], eps, ALU.add).then_inc(step, 1)
                pool.wait_ge(step, nth(b, n, 3))
                tt(row[5], row[3], row[4], ALU.add).then_inc(step, 1)
                pool.wait_ge(step, nth(b, n, 4))
                tt(row[1], row[5], mhalf, ALU.pow).then_inc(step, 1)
                pool.wait_ge(step, nth(b, n, 5))
                tt(row[3], row[1], row[0], ALU.mult).then_inc(step, 1)
                pool.wait_ge(step, nth(b, n, 6))
                return tt(row[2], row[3], mhalf, ALU.mult)

            def ln1(b):
                pool.wait_ge(ln1_stats, nth(b, 1, 1))
                if b[1] is None and b[0] == 0:
                    pool.wait_ge(h_made, CHUNKS)
                else:
                    pool.wait_ge(ln2_transposed, nth(b, 1, 0))
                rstd(bn6, rs1, pool_step1, b).then_inc(ln1_rstd, 1)
                pool.wait_ge(ln1_rstd, nth(b, 1, 1))
                x3 = xtok[0:TS, :].rearrange("p (s d) -> p s d", d=D)
                l3 = lntok[0:TS, :].rearrange("p (s d) -> p s d", d=D)
                gp.tensor_tensor(l3, x3, rs1[0:TS, 1, :].unsqueeze(2).to_broadcast([TS, SUBS, D]), ALU.mult)\
                    .then_inc(ln1_scaled, 1)
                pool.wait_ge(ln1_scaled, nth(b, 1, 1))
                gp.tensor_tensor(l3, l3, rs1[0:TS, 2, :].unsqueeze(2).to_broadcast([TS, SUBS, D]), ALU.add)\
                    .then_inc(ln1_normed, 1)

            def ffn(p):
                xb = xt[:, p[0] % 2, :]
                pool.wait_ge(relu_made, nth(p, 1, 1))
                pool.wait_ge(xt_loaded, nth(p, 16, 16))
                gp.tensor_tensor(xb, xb, relu_ln1[:, 0:UB], ALU.add).then_inc(x1_made, 1)
                pool.wait_ge(ln2_stats, nth(p, 1, 1))
                rstd(bn6b, rs2, pool_step2, p).then_inc(ln2_rstd, 1)
                pool.wait_ge(z_made, nth(p, 1, 1))
                gp.tensor_tensor(bitem[0:TS, 2 * SUBS * E:3 * SUBS * E], ebase[0:TS, :], zz[0:TS, :],
                                 ALU.pow).then_inc(ez_made, 1)

            for i, value in enumerate((1.0 / D, 0.25, EPS, -0.5)):
                gp.memset(consts[:, i, :], value).then_inc(consts_set, 1)
            gp.memset(ebase[:, :], 2.718281828459045).then_inc(consts_set, 1)
            pool.wait_ge(consts_set, 5)
            ln1((0, None))
            ffn((0, None))
            ln1((1, None))
            with pool.Fori(0, (BLOCKS - 2) // 2) as t:
                ffn((1, t))
                ln1((2, t))
                ffn((2, t))
                ln1((3, t))
            ffn((BLOCKS - 1, None))



def kernel(**inputs):
    import numpy as np
    import concourse.bacc as bacc
    from concourse.bass_utils import run_bass_kernel_spmd as run

    def f(name):
        return np.asarray(inputs[name])

    cut = KT * P
    adj = f("adj")
    a = adj[:, :cut].reshape(BLOCKS, UB, CHUNKS, KC, P).transpose(2, 0, 4, 3, 1)
    a = np.ascontiguousarray(a).reshape(CHUNKS, BLOCKS, P, KC * UB)
    at = adj[:, cut:].reshape(BLOCKS, UB, TAIL).transpose(0, 2, 1)
    tail = np.zeros((BLOCKS, TAILP, UB), np.float32)
    x = f("x")
    xtok = np.zeros((BLOCKS, P, SUBS, D), np.float32)
    xtok[:, :TS] = x.reshape(BLOCKS, SUBS, TS, D).transpose(0, 2, 1, 3)
    feat = f("L0_gnn_item_feat")
    feat_tail = np.zeros((P, TAILP), np.float32)
    for r in (0, 32, 64):
        tail[:, r:r + TAIL] = at
        feat_tail[:, r:r + TAIL] = feat[cut:].T
    n_feat = CHUNKS // FEAT
    sel = np.zeros((2 * E, E, P), np.float32)
    for e in range(E):
        sel[[e, E + e], e] = 1.0
    tri = np.tile((np.arange(E)[None, :] < np.arange(E)[:, None]).astype(np.float32), (P, 1, 1))
    arrays = {
        "adj": a,
        "adj_tail": tail,
        "x_tok": xtok.reshape(BLOCKS, P, SUBS * D),
        "x_t": x.reshape(BLOCKS, UB, D).transpose(0, 2, 1),
        "feat_t": feat[:cut].reshape(n_feat, cut // n_feat, D).transpose(0, 2, 1),
        "feat_tail": feat_tail,
        "wi_t": f("L0_gnn_W_item").T,
        "b_item": np.tile(f("L0_gnn_b_item"), (P, KC)),
        "wu_t": f("L0_gnn_W_user").T,
        "b_user": f("L0_gnn_b_user").reshape(D, 1),
        "gate_w": f("L0_ffn_gate_w"),
        "gate_b": np.tile(f("L0_ffn_gate_b"), (P, SUBS)),
        "w1": f("L0_ffn_W1").transpose(1, 0, 2).reshape(D, E * HID),
        "b1": f("L0_ffn_b1").reshape(E * HALVES, P).T,
        "w2": f("L0_ffn_W2").reshape(E, HALVES, P, D).transpose(2, 0, 1, 3).reshape(P, E * HALVES * D),
        "b2": np.tile(f("L0_ffn_b2"), (2, 1)),
        "ident": np.eye(P, dtype=np.float32),
        "sel": sel.reshape(2 * E, E * P),
        "tri": tri,
    }
    arrays = {k: np.ascontiguousarray(v) for k, v in arrays.items()}
    nc = bacc.Bacc("TRN2", target_bir_lowering=False, num_devices=1)
    args = [nc.dram_tensor(k, v.shape, F32, kind="ExternalInput").ap() for k, v in arrays.items()]
    out = nc.dram_tensor("out", (BLOCKS, D, UB), F32, kind="ExternalOutput").ap()
    build(nc, *args, out)
    r = run(nc, [arrays], core_ids=[0])
    return np.ascontiguousarray(r.results[0]["out"].transpose(0, 2, 1)).reshape(N_USER, D)
```
